# Optimizing a Trainium2 kernel written in Bass

```python
import numpy as np
import jax
import jax.numpy as jnp

def _softmax(x, axis=-1):
    return jax.nn.softmax(x, axis=axis)

def _gelu(x):
    return jax.nn.gelu(x, approximate=True)

def _silu(x):
    return jax.nn.silu(x)

def _sigmoid(x):
    return jax.nn.sigmoid(x)

def _layernorm(x, axis=-1, eps=1e-05):
    m = jnp.mean(x, axis=axis, keepdims=True)
    v = jnp.var(x, axis=axis, keepdims=True)
    return (x - m) / jnp.sqrt(v + eps)

def _scatter_add(tgt, idx, src, axis=0):
    return tgt.at[idx].add(src)

def _segment_sum(src, seg, n):
    return jax.ops.segment_sum(src, seg, n)
kernel_name = 'mk_gnn_preln_d1_gnn_r8_4a04e2'

def setup_inputs(seed: int=0):
    np.random.seed(seed)
    _w = jnp.asarray

    def _rec_inputs():
        import jax
        import jax.numpy as jnp
        _gk = jax.random.key(seed)
        x = -0.0003713 + 1 * jax.random.normal(jax.random.fold_in(_gk, 1), (12500, 128), jnp.float32)
        src = jax.random.randint(jax.random.fold_in(_gk, 2), (200000,), 0, 12500, jnp.int32)
        dst = jnp.minimum((12500 * jax.random.uniform(jax.random.fold_in(_gk, 3), (200000,)) ** 2.0).astype(jnp.int32), 99999)
        _o = jnp.argsort(dst, stable=True)
        src = src[_o]
        dst = dst[_o]
        edge_type_4 = jax.random.randint(jax.random.fold_in(_gk, 12), (200000,), 0, 4, jnp.int32)
        return (x, src, dst, edge_type_4)
    x, src, dst, edge_type_4 = _rec_inputs()

    def _L0_gnn_setup():
        import jax, jax.numpy as jnp
        import numpy as np
        N_NODES = 12500
        N_EDGES = 75000
        IN_FEATS = 128
        OUT_FEATS = 128
        N_ETYPES = 4
        key = jax.random.key(seed)
        k_x, k_ei, k_et, k_w, k_b = jax.random.split(key, 5)
        x = jax.random.normal(k_x, (N_NODES, IN_FEATS), dtype=jnp.float32)
        edge_index = jax.random.randint(k_ei, (2, N_EDGES), 0, N_NODES, dtype=jnp.int64)
        edge_types = jax.random.randint(k_et, (N_EDGES,), 0, N_ETYPES, dtype=jnp.int64)
        W = jax.random.normal(k_w, (N_ETYPES, IN_FEATS, OUT_FEATS), dtype=jnp.float32) * (1.0 / np.sqrt(IN_FEATS))
        b = jax.random.normal(k_b, (N_ETYPES, OUT_FEATS), dtype=jnp.float32) * 0.01
        return {'x': x, 'edge_index': edge_index, 'edge_types': edge_types, 'W': W, 'b': b}
    _L0_gnn_all = _L0_gnn_setup()
    _L0_gnn_in = {k: v for k, v in _L0_gnn_all.items() if k in ('W', 'b')}
    del _L0_gnn_all
    return {'x': x, 'src': src, 'dst': dst, 'edge_type_4': edge_type_4, 'L0_gnn_W': _L0_gnn_in['W'], 'L0_gnn_b': _L0_gnn_in['b']}

def reference(x, src, dst, edge_type_4, L0_gnn_W, L0_gnn_b):
    import jax
    import jax.numpy as jnp

    def _L0_gnn_ref(x, edge_index, edge_types, W, b):
        import jax, jax.numpy as jnp
        import numpy as np
        N_NODES = 12500
        N_EDGES = 75000
        IN_FEATS = 128
        OUT_FEATS = 128
        N_ETYPES = 4
        N = x.shape[0]
        src, dst = (edge_index[0], edge_index[1])
        xs = x[src]
        msgs = jnp.zeros((xs.shape[0], W.shape[2]), dtype=x.dtype)
        for i in range(W.shape[0]):
            mask = (edge_types == i)[:, None]
            msgs = msgs + jnp.where(mask, xs @ W[i] + b[i], 0.0)
        out = jax.ops.segment_sum(msgs, dst, num_segments=N)
        return out
    edge_index = jnp.stack([src, dst])
    h = jnp.maximum(_layernorm(x, axis=-1), 0.0)
    x = x + _L0_gnn_ref(h, edge_index, edge_type_4, L0_gnn_W, L0_gnn_b)
    return x

_drawn_inputs = setup_inputs


def setup_inputs(seed=0):
    import zlib

    import numpy as np

    out = dict(_drawn_inputs(seed))
    spreads = {}
    factors = {'L0_gnn_b': 2.754}
    for name, (base, spread) in spreads.items():
        noise = np.random.default_rng([zlib.crc32(name.encode()), seed]).standard_normal(out[name].shape)
        drawn = base * np.exp(spread * noise) if base else spread * noise
        out[name] = jnp.asarray(drawn.astype(out[name].dtype))
    for name, factor in factors.items():
        out[name] = (out[name] * factor).astype(out[name].dtype)
    return out
```

```python
import concourse.bass as bass
import numpy as np
from concourse import mybir

F32 = mybir.dt.float32
I32 = mybir.dt.int32
ALU = mybir.AluOpType
ACT = mybir.ActivationFunctionType
AX = mybir.AxisListType

P = 128
EPS = 1e-5
SB_TILES = 8
SLOTS = 3
EARLY_SBS = 15
GROUP = 14
STATS_STEPS = 10
Y_SLOTS = 7


def gnn_program(nc, x, src, dst, etype, w, b, out, table):
    n_nodes, d = x.shape
    n_edges = src.shape[0]
    n_types = w.shape[0]
    ydim = n_types * d
    node_tiles = -(-n_nodes // P)
    full_node_tiles = n_nodes // P
    node_tail = n_nodes - full_node_tiles * P
    edge_tiles = -(-n_edges // P)
    full_edge_tiles = n_edges // P
    edge_tail = n_edges - full_edge_tiles * P
    groups = node_tiles // GROUP
    full_chunks = full_edge_tiles // P
    tail_rows = full_edge_tiles - full_chunks * P
    chunks = 2 * groups
    sb_per_chunk = P // SB_TILES
    full_sbs = edge_tiles // SB_TILES
    last_tiles = edge_tiles - full_sbs * SB_TILES
    rounds = (full_sbs - EARLY_SBS) // SLOTS
    early_tiles = EARLY_SBS * SB_TILES
    pad_dst = node_tiles * P - 1
    type_step = 1 << pad_dst.bit_length()
    assert d == P and n_types * P == 512 and node_tiles % GROUP == 0 and GROUP % Y_SLOTS == 0 and GROUP % 2 == 0
    assert rounds * SLOTS + EARLY_SBS == full_sbs and last_tiles and edge_tail and node_tail
    assert full_chunks < chunks and early_tiles <= P and pad_dst >= n_nodes and n_types * type_step < 1 << 24

    def sb(name, shape, dt=F32):
        return nc.alloc_sbuf_tensor(name, shape, dt)

    def ps(name, shape):
        return nc.alloc_psum_tensor(name, shape, F32)

    def sem(name):
        return nc.alloc_semaphore(name)

    acc = sb("acc", [P, node_tiles, d])
    table_row = sb("table_row", [P, chunks, P], I32)
    dst_col = sb("dst_col", [P, chunks, P])
    ident = sb("ident", [P, P])
    node_iota = sb("node_iota", [P, P])
    tile_base = sb("tile_base", [P, node_tiles])
    key_iota = sb("key_iota", [P, n_types, P])
    w_sb = sb("w_sb", [d, n_types, d])
    eps = sb("eps", [P, 1])

    src_rows = sb("src_rows", [P, chunks, P], I32)
    type_rows = sb("type_rows", [P, chunks, P], I32)
    dst_rows = sb("dst_rows", [P, chunks, P], I32)
    index_f = sb("index_f", [P, 4, P])
    early_f = sb("early_f", [P, 2, P])
    lohi = sb("lohi", [P, 2, chunks])
    lohi_sb = sb("lohi_sb", [chunks, 2, sb_per_chunk], I32)
    ranges_by_chunk = sb("ranges_by_chunk", [chunks, sb_per_chunk, 4], I32)
    ranges = sb("ranges", [1, chunks, sb_per_chunk * 4], I32)

    bias = sb("bias", [P, ydim])
    stats = sb("stats", [P, GROUP, 6])
    mean_var = sb("mean_var", [P, GROUP, 2])
    std = sb("std", [P, groups, GROUP])
    rstd = sb("rstd", [P, groups, GROUP])
    shift = sb("shift", [P, groups, GROUP])
    h = sb("h", [P, 2, d])
    h_t = sb("h_t", [P, 2, P])
    y = sb("y", [P, Y_SLOTS, ydim])

    src_col = sb("src_col", [P, early_tiles], I32)
    type_col = sb("type_col", [P, early_tiles])
    key_col = sb("key_col", [P, early_tiles])
    early_x = sb("early_x", [P, early_tiles, d])
    e_stats = sb("e_stats", [P, SB_TILES, 6])
    e_mean_var = sb("e_mean_var", [P, SB_TILES, 2])
    e_std = sb("e_std", [P, SB_TILES])
    e_rstd = sb("e_rstd", [P, SB_TILES])
    e_shift = sb("e_shift", [P, SB_TILES])
    y_flat = y[:, :, :].rearrange("p k f -> p (k f)")
    e_h = y_flat[:, 0:SB_TILES * d].rearrange("p (t f) -> p t f", f=d)
    key_onehot = y_flat[:, SB_TILES * d:SB_TILES * d + 4 * ydim].rearrange("p (u t f) -> p u t f", u=2, t=2)
    assert SB_TILES * d + 4 * ydim <= Y_SLOTS * ydim
    type_mask = sb("type_mask", [P, SB_TILES, P])
    h_sums = sb("h_sums", [d, n_types, P])
    edge_counts = sb("edge_counts", [P, P])
    b_rows = sb("b_rows", [P, d])

    row_stage = sb("row_stage", [P, SLOTS, SB_TILES], I32)
    messages = sb("messages", [P, SLOTS, SB_TILES, d])
    onehot = sb("onehot", [P, SB_TILES, P])

    ps_t = ps("ps_t", [P, 2, 512])
    ps_y = ps("ps_y", [P, 2, 512])
    ps_sum = ps("ps_sum", [P, 2, 512])
    ps_i = ps("ps_i", [P, 4, P])

    loaded_src0 = sem("loaded_src0")
    loaded_types0 = sem("loaded_types0")
    loaded_edges = sem("loaded_edges")
    loaded_w = sem("loaded_w")
    loaded_x = [sem(f"loaded_x{g}") for g in range(2)] + [sem("loaded_x_rest")]
    consts = sem("consts")
    own_steps = sem("own_steps")
    pads_set = sem("pads_set")
    dve_consts = sem("dve_consts")
    early_f_ready = sem("early_f_ready")
    early_transposed = sem("early_transposed")
    early_cols = sem("early_cols")
    index_f_ready = sem("index_f_ready")
    lohi_ready = sem("lohi_ready")
    index_transposed = sem("index_transposed")
    index_cols = sem("index_cols")
    lohi_transposed = sem("lohi_transposed")
    ranges_made = sem("ranges_made")
    ranges_ready = sem("ranges_ready")
    stats_taken = sem("stats_taken")
    mean_var_ready = sem("mean_var_ready")
    std_ready = sem("std_ready")
    rstd_ready = sem("rstd_ready")
    norm_ready = sem("norm_ready")
    h_ready = sem("h_ready")
    h_transposed = sem("h_transposed")
    h_t_ready = sem("h_t_ready")
    y_done = sem("y_done")
    y_ready = sem("y_ready")
    y_stored = [sem(f"y_stored{k}") for k in range(Y_SLOTS)]
    stage_ready = sem("stage_ready")
    slots_taken = sem("slots_taken")
    slot_free = [sem(f"slot_free{k}") for k in range(SLOTS)]
    gathered = [sem(f"gathered{k}") for k in range(SLOTS)]
    early_gathered = sem("early_gathered")
    e_stats_taken = sem("e_stats_taken")
    e_mean_var_ready = sem("e_mean_var_ready")
    e_std_ready = sem("e_std_ready")
    e_rstd_ready = sem("e_rstd_ready")
    e_norm_ready = sem("e_norm_ready")
    e_h_ready = sem("e_h_ready")
    e_mask_ready = sem("e_mask_ready")
    e_used = sem("e_used")
    key_onehot_ready = sem("key_onehot_ready")
    key_onehot_free = sem("key_onehot_free")
    h_sums_done = sem("h_sums_done")
    h_sums_ready = sem("h_sums_ready")
    onehot_ready = sem("onehot_ready")
    half_free = sem("half_free")
    pair_added = sem("pair_added")
    acc_final = sem("acc_final")
    stored = sem("stored")

    flat_ranges = ranges[:, :, :].rearrange("p c s -> p (c s)")
    flat_rows = table_row[:, :, :].rearrange("p c t -> p (c t)")
    flat_dst = dst_col[:, :, :].rearrange("p c t -> p (c t)")
    flat_acc = acc[:, :, :].rearrange("p n f -> p (n f)")
    flat_early = early_x[:, :, :].rearrange("p t f -> p (t f)")
    flat_shift = shift[:, :, :].rearrange("p g n -> p (g n)")
    flat_rstd = rstd[:, :, :].rearrange("p g n -> p (g n)")
    w_flat = w_sb[:, :, :].rearrange("i t o -> i (t o)")
    table_rows = table.rearrange("n (t f) -> (n t) f", f=d)
    chunk_edges = P * P
    max_pairs = full_sbs * node_tiles + node_tiles

    def halves(tiles):
        return (0, -(-tiles // 2)), (-(-tiles // 2), tiles)

    def wait(eng, signal, value):
        if not isinstance(value, int) or value > 0:
            eng.wait_ge(signal, value)

    def load_range(eng, s):
        regs = [eng.alloc_register(f"{eng.engine.name}_{n}_{nc.next_id()}") for n in ("lo", "hi")]
        eng.reg_load(regs, flat_ranges[0:1, bass.ds(s * 4, 2)])
        return (eng.snap(regs[0], min_val=0, max_val=node_tiles - 1),
                eng.snap(regs[1], min_val=1, max_val=node_tiles), regs)

    def counter(eng, name):
        reg = eng.alloc_register(f"{eng.engine.name}_{name}")
        eng.reg_mov(reg, 0)
        return reg, lambda: eng.snap(reg, min_val=0, max_val=max_pairs)

    def groups_of(eng, group):
        group(0, False)
        with eng.Fori(1, groups - 1) as g:
            group(g, False)
        group(groups - 1, True)

    with nc.Block() as block:

        @block.sync
        def _(sp):
            lists = ((src_rows, src), (type_rows, etype), (dst_rows, dst))
            first = lists[0][0]
            sp.dma_start(first[:, 0, :], src[0:chunk_edges].rearrange("(r e) -> r e", e=P)).then_inc(loaded_src0, 16)
            for rows, dram in lists[1:]:
                sp.dma_start(rows[:, 0, :], dram[0:chunk_edges].rearrange("(r e) -> r e", e=P)).then_inc(loaded_types0, 16)
            sp.wait_ge(pads_set, 3)
            for rows, dram in lists:
                at = full_chunks * chunk_edges
                sp.dma_start(rows[:, 1:full_chunks, :],
                             dram[chunk_edges:at].rearrange("(c r e) -> r c e", r=P, e=P)).then_inc(loaded_edges, 16)
                sp.dma_start(rows[0:tail_rows, full_chunks, :],
                             dram[at:at + tail_rows * P].rearrange("(r e) -> r e", e=P)).then_inc(loaded_edges, 16)
                at += tail_rows * P
                sp.dma_start(rows[tail_rows:tail_rows + 1, full_chunks, 0:edge_tail],
                             dram[at:at + edge_tail].rearrange("(r e) -> r e", r=1)).then_inc(loaded_edges, 16)
            with sp.Fori(0, node_tiles // Y_SLOTS) as i:
                for k in range(Y_SLOTS):
                    n = i * Y_SLOTS + k
                    sp.wait_ge(y_ready, n + 3)
                    sp.dma_start(table[bass.ds(n * P, P), :], y[:, k, :]).then_inc(y_stored[k], 16)
            sp.wait_ge(ranges_made, 1)
            sp.dma_start(ranges[:, :, :], ranges_by_chunk[:, :, :].rearrange("c s k -> c (s k)")).then_inc(ranges_ready, 16)
            sp.wait_ge(acc_final, 1)
            half = full_node_tiles // 2
            for a, z in ((0, half), (half, full_node_tiles)):
                sp.dma_start(out[a * P:z * P, :].rearrange("(n p) f -> p n f", p=P), acc[:, a:z, :]).then_inc(stored, 16)
            sp.dma_start(out[full_node_tiles * P:n_nodes, :], acc[0:node_tail, full_node_tiles, :]).then_inc(stored, 16)
            sp.wait_ge(stored, 3 * 16)

        @block.gpsimd
        def _(pool):
            pool.memset(ident[:, :], 0.0).then_inc(consts, 1)
            pool.wait_ge(consts, 1)
            pool.affine_select(out=ident[:, :], in_=ident[:, :], compare_op=ALU.not_equal, fill=1.0,
                               base=0, pattern=[[-1, P]], channel_multiplier=1).then_inc(consts, 1)
            pool.iota(node_iota[:, :], pattern=[[1, P]], base=0, channel_multiplier=0,
                      allow_small_or_imprecise_dtypes=True).then_inc(consts, 1)
            pool.iota(tile_base[:, :], pattern=[[P, node_tiles]], base=0, channel_multiplier=0,
                      allow_small_or_imprecise_dtypes=True).then_inc(consts, 1)
            pool.iota(key_iota[:, :, :], pattern=[[type_step, n_types], [1, P]], base=0, channel_multiplier=0,
                      allow_small_or_imprecise_dtypes=True).then_inc(consts, 1)
            pool.wait_ge(early_cols, 1)
            for t in range(early_tiles):
                pool.indirect_dma_start(early_x[:, t, :], None, x,
                                        bass.IndirectOffsetOnAxis(ap=src_col[:, t:t + 1], axis=0)).then_inc(early_gathered, 16)
            for k in range(Y_SLOTS):
                pool.wait_ge(y_stored[k], 16 * node_tiles // Y_SLOTS)

            def gather(k, tiles):
                for t in range(tiles):
                    pool.indirect_dma_start(
                        messages[:, k, t, :], None, table_rows,
                        bass.IndirectOffsetOnAxis(ap=row_stage[:, k, t:t + 1], axis=0)).then_inc(gathered[k], 16)

            with pool.Fori(0, rounds) as i:
                for k in range(SLOTS):
                    pool.wait_ge(stage_ready, i * SLOTS + (k + 1))
                    pool.sem_inc(slots_taken, 1)
                    gather(k, SB_TILES)
            pool.wait_ge(stage_ready, rounds * SLOTS + 1)
            gather(0, last_tiles)

        @block.scalar
        def _(act):
            def load_x(a, z, signal):
                act.dma_start(acc[:, a:z, :], x[a * P:z * P, :].rearrange("(n p) f -> p n f", p=P)).then_inc(signal, 16)

            load_x(0, GROUP, loaded_x[0])
            act.dma_start(w_sb[:, :, :], w.rearrange("t i o -> i t o")).then_inc(loaded_w, 16)
            act.dma_start(bias[:, :], b.rearrange("(a t) o -> a (t o)", a=1).broadcast_to([P, ydim])).then_inc(loaded_w, 16)
            load_x(GROUP, 2 * GROUP, loaded_x[1])
            for g in range(2, groups):
                load_x(g * GROUP, min((g + 1) * GROUP, full_node_tiles), loaded_x[2])
            act.wait_ge(dve_consts, 3)
            act.dma_start(acc[0:node_tail, full_node_tiles, :], x[full_node_tiles * P:n_nodes, :]).then_inc(loaded_x[2], 16)
            act.dma_start(b_rows[0:n_types, :], b).then_inc(loaded_w, 16)

            def make_std(g):
                act.wait_ge(mean_var_ready, (g + 1) * GROUP)
                nc.scalar.activation(std[:, g, :] if isinstance(g, int) else std[:, bass.ds(g, 1), :].rearrange("p a n -> p (a n)"),
                                     mean_var[:, :, 1], ACT.Sqrt,
                                     bias=eps[:, 0:1]).then_inc(std_ready, 1)

            def make_h(n, k):
                act.wait_ge(h_transposed, n)
                nc.scalar.activation(h[:, k, :], flat_acc[:, bass.ds(n * d, d)], ACT.Relu,
                                     bias=flat_shift[:, bass.ds(n, 1)],
                                     scale=flat_rstd[:, bass.ds(n, 1)]).then_inc(h_ready, 1)

            def index_columns(g):
                act.wait_ge(index_transposed, (g + 1) * 4)
                nc.scalar.copy(table_row[:, bass.ds(g * 2, 2), :], ps_i[:, 0:2, :])
                nc.scalar.copy(dst_col[:, bass.ds(g * 2, 2), :], ps_i[:, 2:4, :]).then_inc(index_cols, 1)

            make_std(0)
            act.wait_ge(norm_ready, 1)
            nc.scalar.activation(h[:, 0, :], acc[:, 0, :], ACT.Relu, bias=flat_shift[:, 0:1],
                                 scale=flat_rstd[:, 0:1]).then_inc(h_ready, 1)

            def act_group(g, last):
                for i in range(GROUP):
                    n = g * GROUP + i
                    if i < GROUP - 1:
                        make_h(n + 1, (i + 1) % 2)
                    elif not last:
                        act.wait_ge(norm_ready, g + 2)
                        make_h(n + 1, (i + 1) % 2)
                    act.wait_ge(h_transposed, n + 2)
                    act.wait_ge(y_done, n + 1)
                    nc.scalar.copy(h_t[:, i % 2, :], ps_t[:, i % 2, 0:P]).then_inc(h_t_ready, 1)
                    if i == STATS_STEPS and not last:
                        make_std(g + 1)
                index_columns(g)

            groups_of(act, act_group)

            def stage_rows(i, k, tiles=SB_TILES):
                act.wait_ge(slot_free[k], i + 1)
                nc.scalar.copy(row_stage[:, k, 0:tiles],
                               flat_rows[:, bass.ds((EARLY_SBS + i * SLOTS + k) * SB_TILES, tiles)]).then_inc(stage_ready, 1)

            act.wait_ge(index_cols, groups + 1)
            for k in range(SLOTS):
                stage_rows(0, k)
            act.wait_ge(ranges_ready, 16)
            pair_reg, pair = counter(act, "early_pair")
            with act.Fori(0, EARLY_SBS) as i:
                act.wait_ge(e_mean_var_ready, (i + 1) * SB_TILES)
                nc.scalar.activation(e_std[:, :], e_mean_var[:, :, 1], ACT.Sqrt, bias=eps[:, 0:1]).then_inc(e_std_ready, 1)
                act.wait_ge(e_norm_ready, i + 1)
                act.wait_ge(e_used, i + 1)
                for t in range(SB_TILES):
                    nc.scalar.activation(e_h[:, t, :], flat_early[:, bass.ds((i * SB_TILES + t) * d, d)], ACT.Relu,
                                         bias=e_shift[:, t:t + 1], scale=e_rstd[:, t:t + 1]).then_inc(e_h_ready, 1)
                for k in range(SLOTS):
                    stage_rows(i + 1, k)
                lo, hi, regs = load_range(act, i)
                with act.Fori(lo, hi):
                    p = pair()
                    act.wait_ge(h_sums_done, p + 1)
                    nc.scalar.copy(h_sums[:, :, :], ps_y[:, 0, :].rearrange("f (t n) -> f t n", n=P))
                    nc.scalar.copy(edge_counts[:, :], ps_y[:, 1, 0:P]).then_inc(h_sums_ready, 1)
                    act.reg_add(pair_reg, pair_reg, 1)
                for r in regs:
                    act.free_register(r)
            with act.Fori(EARLY_SBS + 1, rounds) as i:
                for k in range(SLOTS):
                    stage_rows(i, k)
            stage_rows(rounds, 0, last_tiles)

        @block.vector
        def _(dve):
            nc.vector.memset(eps[:, :], EPS).then_inc(dve_consts, 1)
            nc.vector.memset(acc[:, full_node_tiles, :], 0.0).then_inc(dve_consts, 1)
            nc.vector.memset(b_rows[:, :], 0.0).then_inc(dve_consts, 1)
            nc.vector.memset(dst_rows[:, full_chunks:chunks, :], pad_dst).then_inc(pads_set, 1)
            nc.vector.memset(src_rows[:, full_chunks:chunks, :], 0).then_inc(pads_set, 1)
            nc.vector.memset(type_rows[:, full_chunks:chunks, :], 0).then_inc(pads_set, 1)
            dve.wait_ge(loaded_src0, 16)
            nc.vector.tensor_copy(early_f[:, 0, :], src_rows[:, 0, :]).then_inc(early_f_ready, 1)
            dve.wait_ge(early_transposed, 1)
            nc.vector.tensor_copy(src_col[:, :], ps_i[:, 0, 0:early_tiles]).then_inc(early_cols, 1)
            dve.wait_ge(loaded_types0, 32)
            nc.vector.tensor_copy(early_f[:, 1, :], type_rows[:, 0, :]).then_inc(early_f_ready, 1)
            dve.sem_inc(y_ready, 2)

            def take_stats(g, i):
                n = g * GROUP + i
                nc.vector.bn_stats(stats[:, i, :], flat_acc[:, bass.ds(n * d, d)]).then_inc(stats_taken, 1)

            def join_stats(i):
                nc.vector.bn_aggr(mean_var[:, i, :], stats[:, i, :]).then_inc(mean_var_ready, 1)

            def make_norm(g):
                dve.wait_ge(std_ready, g + 1)
                nc.vector.reciprocal(rstd[:, bass.ds(g, 1), :], std[:, bass.ds(g, 1), :]).then_inc(rstd_ready, 1)
                dve.wait_ge(rstd_ready, g + 1)
                nc.vector.scalar_tensor_tensor(out=shift[:, bass.ds(g, 1), :], in0=mean_var[:, :, 0].unsqueeze(1),
                                               scalar=-1.0, in1=rstd[:, bass.ds(g, 1), :],
                                               op0=ALU.mult, op1=ALU.mult).then_inc(norm_ready, 1)

            def index_to_f32(g):
                two = bass.ds(g * 2, 2)
                wait(dve, index_transposed, g * 4)
                nc.vector.scalar_tensor_tensor(out=index_f[:, 0:2, :], in0=src_rows[:, two, :], scalar=float(n_types),
                                               in1=type_rows[:, two, :], op0=ALU.mult, op1=ALU.add).then_inc(index_f_ready, 1)
                nc.vector.tensor_copy(index_f[:, 2:4, :], dst_rows[:, two, :]).then_inc(index_f_ready, 1)
                nc.vector.tensor_reduce(lohi[:, 0, two], dst_rows[:, two, :], AX.X, ALU.min).then_inc(lohi_ready, 1)
                nc.vector.tensor_reduce(lohi[:, 1, two], dst_rows[:, two, :], AX.X, ALU.max).then_inc(lohi_ready, 1)

            dve.wait_ge(loaded_x[0], 16)
            for i in range(GROUP):
                take_stats(0, i)
            dve.wait_ge(stats_taken, GROUP)
            for i in range(GROUP):
                join_stats(i)
            make_norm(0)
            dve.wait_ge(loaded_w, 48)

            def dve_group(g, last):
                first = isinstance(g, int) and g == 0
                if first:
                    dve.wait_ge(loaded_x[1], 16)
                elif not last:
                    dve.wait_ge(loaded_x[2], 16 * (groups - 1))
                if first:
                    dve.wait_ge(loaded_edges, 16 * 9)
                for i in range(GROUP):
                    n = g * GROUP + i
                    if i == STATS_STEPS + 2 and not last:
                        make_norm(g + 1)
                    joined = []
                    if not last and i <= STATS_STEPS:
                        for m in range(i * GROUP // STATS_STEPS, min((i + 1) * GROUP // STATS_STEPS, GROUP)):
                            take_stats(g + 1, m)
                        joined = range(max(i - 1, 0) * GROUP // STATS_STEPS, i * GROUP // STATS_STEPS)
                    if joined:
                        dve.wait_ge(stats_taken, (g + 1) * GROUP + joined[-1] + 1)
                    wait(dve, y_stored[i % Y_SLOTS], (g * (GROUP // Y_SLOTS) + i // Y_SLOTS) * 16)
                    dve.wait_ge(y_done, n + 3)
                    nc.vector.tensor_tensor(y[:, i % Y_SLOTS, :], ps_y[:, i % 2, :], bias[:, :], ALU.add).then_inc(y_ready, 1)
                    for m in joined:
                        join_stats(m)
                    if i == STATS_STEPS:
                        index_to_f32(g)

            groups_of(dve, dve_group)

            dve.wait_ge(lohi_transposed, 2)
            for m, op in enumerate((ALU.min, ALU.max)):
                nc.vector.tensor_reduce(lohi_sb[:, m, :], ps_t[0:chunks, m, 0:P].rearrange("c (s t) -> c s t", t=SB_TILES),
                                        AX.X, op).then_inc(own_steps, 1)
            nc.vector.memset(ranges_by_chunk[:, :, :], 0).then_inc(own_steps, 1)
            dve.wait_ge(own_steps, 3)
            nc.vector.tensor_scalar(lohi_sb[:, :, :], lohi_sb[:, :, :], P.bit_length() - 1, None,
                                    ALU.arith_shift_right).then_inc(own_steps, 1)
            dve.wait_ge(own_steps, 4)
            nc.vector.tensor_copy(ranges_by_chunk[:, :, 0], lohi_sb[:, 0, :]).then_inc(own_steps, 1)
            dve.wait_ge(own_steps, 5)
            nc.vector.tensor_scalar_add(ranges_by_chunk[:, :, 1], lohi_sb[:, 1, :], 1.0).then_inc(ranges_made, 1)

            nc.vector.memset(type_mask[:, :, :], 0.0).then_inc(own_steps, 1)
            nc.vector.memset(ps_sum[:, 1, 0:d], 0.0).then_inc(pair_added, 1)
            dve.wait_ge(early_transposed, 2)
            nc.vector.tensor_copy(type_col[:, :], ps_i[:, 0, 0:early_tiles]).then_inc(own_steps, 1)
            dve.wait_ge(own_steps, 7)
            dve.wait_ge(index_cols, groups + 1)
            dve.wait_ge(consts, 5)
            nc.vector.scalar_tensor_tensor(out=key_col[:, :], in0=type_col[:, :], scalar=float(type_step),
                                           in1=dst_col[:, 0, 0:early_tiles], op0=ALU.mult, op1=ALU.add).then_inc(own_steps, 1)
            dve.wait_ge(own_steps, 8)
            dve.wait_ge(ranges_ready, 16)
            dve.wait_ge(early_gathered, 16 * early_tiles)
            for k in range(Y_SLOTS):
                dve.wait_ge(y_stored[k], 16 * node_tiles // Y_SLOTS)
            dve.sem_inc(key_onehot_free, 2)

            q_reg, count = counter(dve, "pair")
            p_reg, early_count = counter(dve, "early_pair")
            before_reg, _ = counter(dve, "tile_before")

            def tile_before():
                return dve.snap(before_reg, min_val=0, max_val=node_tiles - 1)

            def add_sums(q):
                tile = tile_before()
                dve.wait_ge(pair_added, q + 1)
                dve.wait_ge(half_free, q * 2 + 2)
                at = flat_acc[:, bass.ds(tile * d, d)]
                return nc.vector.tensor_tensor(at, at, ps_sum[:, bass.ds((q + 1) % 2, 1), 0:d], ALU.add)

            def superblock(s, tiles, early=False):
                lo, hi, regs = load_range(dve, s)
                with dve.Fori(lo, hi) as j:
                    q = count()
                    for half, (a, z) in enumerate(halves(tiles)):
                        dve.wait_ge(half_free, q * 2 + (half + 1))
                        nc.vector.scalar_tensor_tensor(
                            out=onehot[:, a:z, :],
                            in0=node_iota[:, :].unsqueeze(1).broadcast_to([P, z - a, P]),
                            scalar=tile_base[:, bass.ds(j, 1)],
                            in1=flat_dst[:, bass.ds(s * SB_TILES + a, z - a)].unsqueeze(2).broadcast_to([P, z - a, P]),
                            op0=ALU.add, op1=ALU.is_equal).then_inc(onehot_ready, 1)
                    if early:
                        p = early_count()
                        for u in range(tiles // 2):
                            dve.wait_ge(key_onehot_free, p * (tiles // 2) + (u + 1))
                            nc.vector.scalar_tensor_tensor(
                                out=key_onehot[:, u % 2, :, :],
                                in0=key_iota[:, :, :].rearrange("p t n -> p (t n)").unsqueeze(1).broadcast_to([P, 2, ydim]),
                                scalar=tile_base[:, bass.ds(j, 1)],
                                in1=key_col[:, bass.ds(s * SB_TILES + 2 * u, 2)].unsqueeze(2).broadcast_to([P, 2, ydim]),
                                op0=ALU.add, op1=ALU.is_equal).then_inc(key_onehot_ready, 1)
                        dve.reg_add(p_reg, p_reg, 1)
                    add_sums(q).then_inc(pair_added, 1)
                    dve.reg_mov(before_reg, j)
                    dve.reg_add(q_reg, q_reg, 1)
                for r in regs:
                    dve.free_register(r)

            with dve.Fori(0, EARLY_SBS) as i:
                s = EARLY_SBS + i * SLOTS
                for t in range(SB_TILES):
                    nc.vector.bn_stats(e_stats[:, t, :], flat_early[:, bass.ds((i * SB_TILES + t) * d, d)]).then_inc(e_stats_taken, 1)
                dve.wait_ge(e_stats_taken, (i + 1) * SB_TILES)
                dve.wait_ge(e_used, i + 1)
                nc.vector.tensor_tensor(
                    type_mask[:, :, 0:n_types], node_iota[:, 0:n_types].unsqueeze(1).broadcast_to([P, SB_TILES, n_types]),
                    type_col[:, bass.ds(i * SB_TILES, SB_TILES)].unsqueeze(2).broadcast_to([P, SB_TILES, n_types]),
                    ALU.is_equal).then_inc(e_mask_ready, 1)
                for t in range(SB_TILES):
                    nc.vector.bn_aggr(e_mean_var[:, t, :], e_stats[:, t, :]).then_inc(e_mean_var_ready, 1)
                superblock(s, SB_TILES)
                dve.wait_ge(e_std_ready, i + 1)
                nc.vector.reciprocal(e_rstd[:, :], e_std[:, :]).then_inc(e_rstd_ready, 1)
                dve.wait_ge(e_rstd_ready, i + 1)
                nc.vector.scalar_tensor_tensor(out=e_shift[:, :], in0=e_mean_var[:, :, 0], scalar=-1.0,
                                               in1=e_rstd[:, :], op0=ALU.mult, op1=ALU.mult).then_inc(e_norm_ready, 1)
                superblock(s + 1, SB_TILES)
                superblock(s + 2, SB_TILES)
                superblock(i, SB_TILES, early=True)
            with dve.Fori(EARLY_SBS * (SLOTS + 1), full_sbs) as s:
                superblock(s, SB_TILES)
            superblock(full_sbs, last_tiles)
            add_sums(count()).then_inc(acc_final, 1)

        @block.tensor
        def _(pe):
            pe.wait_ge(consts, 2)
            pe.wait_ge(early_f_ready, 1)
            nc.tensor.transpose(ps_i[:, 0, :], early_f[:, 0, :], ident[:, :]).then_inc(early_transposed, 1)

            def transpose_h(n, k):
                pe.wait_ge(h_ready, n + 1)
                nc.tensor.transpose(ps_t[:, k, 0:P], h[:, k, :], ident[:, :]).then_inc(h_transposed, 1)

            def pe_group(g, last):
                for i in range(GROUP):
                    n = g * GROUP + i
                    if not (last and i == GROUP - 1):
                        transpose_h(n + 1, (i + 1) % 2)
                    pe.wait_ge(h_t_ready, n + 1)
                    pe.wait_ge(y_ready, n + 1)
                    nc.tensor.matmul(ps_y[:, i % 2, :], h_t[:, i % 2, :], w_flat, start=True, stop=True).then_inc(y_done, 1)
                pe.wait_ge(index_f_ready, (g + 1) * 2)
                pe.wait_ge(index_cols, g + 1)
                for m in range(4):
                    nc.tensor.transpose(ps_i[:, m, :], index_f[:, m, :], ident[:, :]).then_inc(index_transposed, 1)

            pe.sem_inc(h_transposed, 1)
            pe.sem_inc(y_done, 2)
            pe.wait_ge(early_cols, 1)
            pe.sem_inc(index_cols, 1)
            pe.wait_ge(loaded_w, 48)
            transpose_h(0, 0)
            groups_of(pe, pe_group)

            pe.wait_ge(h_t_ready, node_tiles)
            pe.wait_ge(lohi_ready, 2 * groups)
            for m in range(2):
                nc.tensor.transpose(ps_t[0:chunks, m, 0:P], lohi[:, m, :], ident[:, :]).then_inc(lohi_transposed, 1)
            pe.wait_ge(early_f_ready, 2)
            pe.wait_ge(index_cols, groups + 1)
            nc.tensor.transpose(ps_i[:, 0, :], early_f[:, 1, :], ident[:, :]).then_inc(early_transposed, 1)

            pe.wait_ge(ranges_ready, 16)
            pe.wait_ge(y_ready, node_tiles + 2)
            for k in range(SLOTS):
                pe.sem_inc(slot_free[k], 1)
            pe.sem_inc(half_free, 2)
            pe.sem_inc(e_used, 1)
            q_reg, count = counter(pe, "pair")
            p_reg, early_count = counter(pe, "early_pair")

            def superblock(s, k, tiles, needed):
                lo, hi, regs = load_range(pe, s)
                with pe.Fori(lo, hi):
                    q = count()
                    pe.wait_ge(gathered[k], needed)
                    pe.wait_ge(pair_added, q + 1)
                    for half, (a, z) in enumerate(halves(tiles)):
                        pe.wait_ge(onehot_ready, q * 2 + (half + 1))
                        for t in range(a, z):
                            ins = nc.tensor.matmul(ps_sum[:, bass.ds(q % 2, 1), 0:d], onehot[:, t, :],
                                                   messages[:, k, t, :], start=(t == 0), stop=(t == tiles - 1))
                        ins.then_inc(half_free, 1)
                    pe.reg_add(q_reg, q_reg, 1)
                pe.wait_ge(half_free, count() * 2 + 2)
                pe.sem_inc(slot_free[k], 1)
                for r in regs:
                    pe.free_register(r)

            def early_superblock(i):
                lo, hi, regs = load_range(pe, i)
                with pe.Fori(lo, hi):
                    q, p = count(), early_count()
                    pe.wait_ge(e_mask_ready, i + 1)
                    for half, (a, z) in enumerate(halves(SB_TILES)):
                        pe.wait_ge(onehot_ready, q * 2 + (half + 1))
                        for t in range(a, z):
                            ins = nc.tensor.matmul(ps_y[:, 1, 0:P], type_mask[:, t, :], onehot[:, t, :],
                                                   start=(t == 0), stop=(t == SB_TILES - 1))
                        if half == 0:
                            ins.then_inc(half_free, 1)
                    pe.wait_ge(e_h_ready, (i + 1) * SB_TILES)
                    for u in range(SB_TILES // 2):
                        pe.wait_ge(key_onehot_ready, p * (SB_TILES // 2) + (u + 1))
                        for t in range(2):
                            ins = nc.tensor.matmul(ps_y[:, 0, :], e_h[:, 2 * u + t, :], key_onehot[:, u % 2, t, :],
                                                   start=(u == 0 and t == 0), stop=(u == SB_TILES // 2 - 1 and t == 1))
                        ins.then_inc(key_onehot_free, 1)
                    pe.wait_ge(key_onehot_free, (p + 1) * (SB_TILES // 2) + 2)
                    pe.sem_inc(h_sums_done, 1)
                    pe.wait_ge(pair_added, q + 1)
                    pe.wait_ge(h_sums_ready, p + 1)
                    for t in range(n_types):
                        nc.tensor.matmul(ps_sum[:, bass.ds(q % 2, 1), 0:d], h_sums[:, t, :], w_sb[:, t, :],
                                         start=(t == 0), stop=False)
                    nc.tensor.matmul(ps_sum[:, bass.ds(q % 2, 1), 0:d], edge_counts[:, :], b_rows[:, :],
                                     start=False, stop=True).then_inc(half_free, 1)
                    pe.reg_add(q_reg, q_reg, 1)
                    pe.reg_add(p_reg, p_reg, 1)
                pe.wait_ge(half_free, count() * 2 + 2)
                pe.sem_inc(e_used, 1)
                for r in regs:
                    pe.free_register(r)

            def table_round(i):
                for k in range(SLOTS):
                    superblock(EARLY_SBS + i * SLOTS + k, k, SB_TILES, (i + 1) * (16 * SB_TILES))

            with pe.Fori(0, EARLY_SBS) as i:
                table_round(i)
                early_superblock(i)
            with pe.Fori(EARLY_SBS, rounds) as i:
                table_round(i)
            superblock(full_sbs, 0, last_tiles, rounds * 16 * SB_TILES + 16 * last_tiles)


_INS = ["x", "src", "dst", "edge_type_4", "L0_gnn_W", "L0_gnn_b"]


def kernel(**inputs):
    import concourse.bacc as _bacc
    from concourse.bass_utils import run_bass_kernel_spmd as _run

    nc = _bacc.Bacc("TRN2", target_bir_lowering=False, num_devices=1)
    arrays, args = {}, []
    for name in _INS:
        a = np.ascontiguousarray(inputs[name])
        arrays[f"in_{name}"] = a
        args.append(nc.dram_tensor(f"in_{name}", a.shape, mybir.dt.from_np(a.dtype), kind="ExternalInput").ap())
    n_nodes, d = inputs["x"].shape
    n_types = inputs["L0_gnn_W"].shape[0]
    args.append(nc.dram_tensor("out", (n_nodes, d), F32, kind="ExternalOutput").ap())
    rows = -(-n_nodes // P) * P
    args.append(nc.dram_tensor("message_table", (rows, n_types * d), F32).ap())
    gnn_program(nc, *args)
    r = _run(nc, [arrays], core_ids=[0])
    return r.results[0]["out"]
```
